# Optimizing a Trainium2 kernel written in Bass

```python
import numpy as np
import jax
import jax.numpy as jnp

def _softmax(x, axis=-1):
    return jax.nn.softmax(x, axis=axis)

def _gelu(x):
    return jax.nn.gelu(x, approximate=True)

def _silu(x):
    return jax.nn.silu(x)

def _sigmoid(x):
    return jax.nn.sigmoid(x)

def _layernorm(x, axis=-1, eps=1e-05):
    m = jnp.mean(x, axis=axis, keepdims=True)
    v = jnp.var(x, axis=axis, keepdims=True)
    return (x - m) / jnp.sqrt(v + eps)

def _scatter_add(tgt, idx, src, axis=0):
    return tgt.at[idx].add(src)

def _segment_sum(src, seg, n):
    return jax.ops.segment_sum(src, seg, n)
kernel_name = 'mk_decoder_postln_d1_seqx_r4_f43d6d'

def setup_inputs(seed: int=0):
    np.random.seed(seed)
    _w = jnp.asarray

    def _rec_inputs():
        import jax
        import jax.numpy as jnp
        _rk = jax.random.key(seed)
        x = 0.000341 + 1 * jax.random.normal(jax.random.fold_in(_rk, 1), (16, 256, 512), jnp.float32)
        _lenS = 256 - jax.random.randint(jax.random.fold_in(_rk, 7), (16,), 0, max(1, 256 // 4) + 1, jnp.int32)
        _lenS2 = 256 - jax.random.randint(jax.random.fold_in(_rk, 8), (16,), 0, max(1, 256 // 4) + 1, jnp.int32)
        _ctx_2048P = jax.random.normal(jax.random.fold_in(_rk, 11), (16, 16, 512), jnp.float32)
        _ctx_2048c = jax.random.dirichlet(jax.random.fold_in(_rk, 511), 0.3 * jnp.ones((16,), jnp.float32), (16, 256))
        _ctx_2048t = jnp.einsum('bsk,bkd->bsd', _ctx_2048c, _ctx_2048P)
        _ctx_2048t = _ctx_2048t * jax.lax.rsqrt(jnp.mean(jnp.square(_ctx_2048t)) + 1e-12) * 0.953939
        ctx_2048 = -1.47943e-05 + 1.00017 * (_ctx_2048t + 0.3 * jax.random.normal(jax.random.fold_in(_rk, 611), (16, 256, 512), jnp.float32))
        return (x, ctx_2048)
    x, ctx_2048 = _rec_inputs()

    def _L0_attn_setup():
        import jax, jax.numpy as jnp
        import numpy as np
        B_, L_, D_ = (2, 256, 512)
        E_, N_, R_, K_ = (1024, 16, 128, 4)
        EPS = 1e-05

        def _forward(resid, norm_w, skip_w, in_w, conv_w, conv_b, wd1, wd2, wd2_b, wB, wC, A_log, W_D, out_w):
            B, L, D = resid.shape
            E, K = conv_w.shape
            N = A_log.shape[1]
            rn = resid * jax.lax.rsqrt(jnp.mean(resid * resid, -1, keepdims=True) + EPS) * norm_w
            skip = rn @ skip_w.T
            x_in = rn @ in_w.T
            xp = jnp.pad(x_in, ((0, 0), (K - 1, 0), (0, 0)))
            conv = conv_b + sum((xp[:, k:k + L, :] * conv_w[:, k] for k in range(K)))
            x = jax.nn.silu(conv)
            delta = jax.nn.softplus(x @ wd1.T @ wd2.T + wd2_b)
            A = -jnp.exp(A_log)
            Bm = x @ wB.T
            Cm = x @ wC.T

            def step(h, inp):
                d_l, b_l, c_l, x_l = inp
                h = jnp.exp(d_l[:, :, None] * A) * h + (d_l * x_l)[:, :, None] * b_l[:, None, :]
                y_l = jnp.einsum('ben,bn->be', h, c_l)
                return (h, y_l)
            h0 = jnp.zeros((B, E, N), resid.dtype)
            xs = (delta.transpose(1, 0, 2), Bm.transpose(1, 0, 2), Cm.transpose(1, 0, 2), x.transpose(1, 0, 2))
            _, ys = jax.lax.scan(step, h0, xs)
            y = ys.transpose(1, 0, 2) + x * W_D
            y = y * jax.nn.silu(skip)
            return resid + y @ out_w.T
        key = jax.random.key(seed)
        ks = jax.random.split(key, 12)
        s = lambda i, shape, scale=0.02: jax.random.normal(ks[i], shape, jnp.float32) * scale
        dt = jnp.exp(jax.random.uniform(ks[10], (E_,)) * (np.log(0.1) - np.log(0.001)) + np.log(0.001))
        inv_dt = dt + jnp.log(-jnp.expm1(-dt))
        return {'resid': jax.random.normal(ks[0], (B_, L_, D_), jnp.float32), 'norm_w': jnp.ones((D_,), jnp.float32), 'skip_w': s(1, (E_, D_)), 'in_w': s(2, (E_, D_)), 'conv_w': s(3, (E_, K_), 0.2), 'conv_b': jnp.zeros((E_,), jnp.float32), 'wd1': s(4, (R_, E_)), 'wd2': s(5, (E_, R_), R_ ** (-0.5)), 'wd2_b': inv_dt, 'wB': s(6, (N_, E_)), 'wC': s(7, (N_, E_)), 'A_log': jnp.log(jnp.broadcast_to(jnp.arange(1, N_ + 1, dtype=jnp.float32), (E_, N_))), 'W_D': jnp.ones((E_,), jnp.float32), 'out_w': s(8, (D_, E_))}
    _L0_attn_all = _L0_attn_setup()
    _L0_attn_in = {k: v for k, v in _L0_attn_all.items() if k in ('norm_w', 'skip_w', 'in_w', 'conv_w', 'conv_b', 'wd1', 'wd2', 'wd2_b', 'wB', 'wC', 'A_log', 'W_D', 'out_w')}
    del _L0_attn_all

    def _L0_xattn_setup():
        import jax, jax.numpy as jnp
        import numpy as np

        def _wkv(time_decay, time_first, k, v):
            w = -jnp.exp(time_decay)
            u = time_first
            B, T, C = k.shape
            aa = jnp.zeros((B, C), dtype=k.dtype)
            bb = jnp.zeros((B, C), dtype=k.dtype)
            pp = jnp.full((B, C), -1e+38, dtype=k.dtype)

            def step(carry, kv_t):
                aa, bb, pp = carry
                kt, vt = kv_t
                ww = u + kt
                q = jnp.maximum(pp, ww)
                e1 = jnp.exp(pp - q)
                e2 = jnp.exp(ww - q)
                y_t = (e1 * aa + e2 * vt) / (e1 * bb + e2)
                ww2 = pp + w
                q2 = jnp.maximum(ww2, kt)
                e1b = jnp.exp(ww2 - q2)
                e2b = jnp.exp(kt - q2)
                new_carry = (e1b * aa + e2b * vt, e1b * bb + e2b, q2)
                return (new_carry, y_t)
            ks = jnp.transpose(k, (1, 0, 2))
            vs = jnp.transpose(v, (1, 0, 2))
            _, ys = jax.lax.scan(step, (aa, bb, pp), (ks, vs))
            return jnp.transpose(ys, (1, 0, 2))
        key = jax.random.key(seed)
        k1, k2, k3, k4 = jax.random.split(key, 4)
        B, T, C = (8, 256, 512)
        return {'batch_size': B, 'seq_len': T, 'embedding_dim': C, 'time_decay': jax.random.normal(k1, (C,), dtype=jnp.float32), 'time_first': jax.random.normal(k2, (C,), dtype=jnp.float32), 'k': jax.random.normal(k3, (B, T, C), dtype=jnp.float32), 'v': jax.random.normal(k4, (B, T, C), dtype=jnp.float32)}
    _L0_xattn_all = _L0_xattn_setup()
    _L0_xattn_in = {k: v for k, v in _L0_xattn_all.items() if k in ('time_decay', 'time_first')}
    del _L0_xattn_all

    def _L0_ffn_setup():
        import jax, jax.numpy as jnp
        import numpy as np
        DIM = 512
        HID = 1408
        ZERO_POINT = 128.0

        def _qlinear(x, wq, scale):
            W = (wq.astype(jnp.float32) - ZERO_POINT) * scale[:, None]
            return jnp.einsum('bsd,hd->bsh', x, W)
        key = jax.random.key(seed)
        ks = jax.random.split(key, 7)
        B, S = (4, 512)
        sg = jax.random.uniform(ks[1], (HID,)) * (0.02 / np.sqrt(DIM)) + 0.0001
        su = jax.random.uniform(ks[3], (HID,)) * (0.02 / np.sqrt(DIM)) + 0.0001
        sd = jax.random.uniform(ks[5], (DIM,)) * (0.02 / np.sqrt(HID)) + 0.0001
        return {'x': jax.random.normal(ks[0], (B, S, DIM), dtype=jnp.float32), 'wq_gate': jax.random.randint(ks[2], (HID, DIM), 0, 64, dtype=jnp.int32), 's_gate': sg, 'wq_up': jax.random.randint(ks[4], (HID, DIM), 0, 64, dtype=jnp.int32), 's_up': su, 'wq_down': jax.random.randint(ks[6], (DIM, HID), 0, 64, dtype=jnp.int32), 's_down': sd}
    _L0_ffn_all = _L0_ffn_setup()
    _L0_ffn_in = {k: v for k, v in _L0_ffn_all.items() if k in ('wq_gate', 's_gate', 'wq_up', 's_up', 'wq_down', 's_down')}
    del _L0_ffn_all
    return {'x': x, 'ctx_2048': ctx_2048, 'L0_attn_norm_w': _L0_attn_in['norm_w'], 'L0_attn_skip_w': _L0_attn_in['skip_w'], 'L0_attn_in_w': _L0_attn_in['in_w'], 'L0_attn_conv_w': _L0_attn_in['conv_w'], 'L0_attn_conv_b': _L0_attn_in['conv_b'], 'L0_attn_wd1': _L0_attn_in['wd1'], 'L0_attn_wd2': _L0_attn_in['wd2'], 'L0_attn_wd2_b': _L0_attn_in['wd2_b'], 'L0_attn_wB': _L0_attn_in['wB'], 'L0_attn_wC': _L0_attn_in['wC'], 'L0_attn_A_log': _L0_attn_in['A_log'], 'L0_attn_W_D': _L0_attn_in['W_D'], 'L0_attn_out_w': _L0_attn_in['out_w'], 'L0_xattn_time_decay': _L0_xattn_in['time_decay'], 'L0_xattn_time_first': _L0_xattn_in['time_first'], 'L0_ffn_wq_gate': _L0_ffn_in['wq_gate'], 'L0_ffn_s_gate': _L0_ffn_in['s_gate'], 'L0_ffn_wq_up': _L0_ffn_in['wq_up'], 'L0_ffn_s_up': _L0_ffn_in['s_up'], 'L0_ffn_wq_down': _L0_ffn_in['wq_down'], 'L0_ffn_s_down': _L0_ffn_in['s_down']}

def reference(x, ctx_2048, L0_attn_norm_w, L0_attn_skip_w, L0_attn_in_w, L0_attn_conv_w, L0_attn_conv_b, L0_attn_wd1, L0_attn_wd2, L0_attn_wd2_b, L0_attn_wB, L0_attn_wC, L0_attn_A_log, L0_attn_W_D, L0_attn_out_w, L0_xattn_time_decay, L0_xattn_time_first, L0_ffn_wq_gate, L0_ffn_s_gate, L0_ffn_wq_up, L0_ffn_s_up, L0_ffn_wq_down, L0_ffn_s_down):
    import jax
    import jax.numpy as jnp

    def _L0_attn_ref(resid, norm_w, skip_w, in_w, conv_w, conv_b, wd1, wd2, wd2_b, wB, wC, A_log, W_D, out_w):
        import jax, jax.numpy as jnp
        import numpy as np
        B_, L_, D_ = (2, 256, 512)
        E_, N_, R_, K_ = (1024, 16, 128, 4)
        EPS = 1e-05

        def _forward(resid, norm_w, skip_w, in_w, conv_w, conv_b, wd1, wd2, wd2_b, wB, wC, A_log, W_D, out_w):
            B, L, D = resid.shape
            E, K = conv_w.shape
            N = A_log.shape[1]
            rn = resid * jax.lax.rsqrt(jnp.mean(resid * resid, -1, keepdims=True) + EPS) * norm_w
            skip = rn @ skip_w.T
            x_in = rn @ in_w.T
            xp = jnp.pad(x_in, ((0, 0), (K - 1, 0), (0, 0)))
            conv = conv_b + sum((xp[:, k:k + L, :] * conv_w[:, k] for k in range(K)))
            x = jax.nn.silu(conv)
            delta = jax.nn.softplus(x @ wd1.T @ wd2.T + wd2_b)
            A = -jnp.exp(A_log)
            Bm = x @ wB.T
            Cm = x @ wC.T

            def step(h, inp):
                d_l, b_l, c_l, x_l = inp
                h = jnp.exp(d_l[:, :, None] * A) * h + (d_l * x_l)[:, :, None] * b_l[:, None, :]
                y_l = jnp.einsum('ben,bn->be', h, c_l)
                return (h, y_l)
            h0 = jnp.zeros((B, E, N), resid.dtype)
            xs = (delta.transpose(1, 0, 2), Bm.transpose(1, 0, 2), Cm.transpose(1, 0, 2), x.transpose(1, 0, 2))
            _, ys = jax.lax.scan(step, h0, xs)
            y = ys.transpose(1, 0, 2) + x * W_D
            y = y * jax.nn.silu(skip)
            return resid + y @ out_w.T
        return _forward(resid, norm_w, skip_w, in_w, conv_w, conv_b, wd1, wd2, wd2_b, wB, wC, A_log, W_D, out_w)

    def _L0_xattn_ref(batch_size, seq_len, embedding_dim, time_decay, time_first, k, v):
        import jax, jax.numpy as jnp
        import numpy as np

        def _wkv(time_decay, time_first, k, v):
            w = -jnp.exp(time_decay)
            u = time_first
            B, T, C = k.shape
            aa = jnp.zeros((B, C), dtype=k.dtype)
            bb = jnp.zeros((B, C), dtype=k.dtype)
            pp = jnp.full((B, C), -1e+38, dtype=k.dtype)

            def step(carry, kv_t):
                aa, bb, pp = carry
                kt, vt = kv_t
                ww = u + kt
                q = jnp.maximum(pp, ww)
                e1 = jnp.exp(pp - q)
                e2 = jnp.exp(ww - q)
                y_t = (e1 * aa + e2 * vt) / (e1 * bb + e2)
                ww2 = pp + w
                q2 = jnp.maximum(ww2, kt)
                e1b = jnp.exp(ww2 - q2)
                e2b = jnp.exp(kt - q2)
                new_carry = (e1b * aa + e2b * vt, e1b * bb + e2b, q2)
                return (new_carry, y_t)
            ks = jnp.transpose(k, (1, 0, 2))
            vs = jnp.transpose(v, (1, 0, 2))
            _, ys = jax.lax.scan(step, (aa, bb, pp), (ks, vs))
            return jnp.transpose(ys, (1, 0, 2))
        assert seq_len <= 256
        return _wkv(time_decay, time_first, k, v)

    def _L0_ffn_ref(x, wq_gate, s_gate, wq_up, s_up, wq_down, s_down):
        import jax, jax.numpy as jnp
        import numpy as np
        DIM = 512
        HID = 1408
        ZERO_POINT = 128.0

        def _qlinear(x, wq, scale):
            W = (wq.astype(jnp.float32) - ZERO_POINT) * scale[:, None]
            return jnp.einsum('bsd,hd->bsh', x, W)
        gate = _qlinear(x, wq_gate, s_gate)
        gate = jax.nn.silu(gate)
        up = _qlinear(x, wq_up, s_up)
        return _qlinear(gate * up, wq_down, s_down)
    x = _layernorm(x + _L0_attn_ref(x, L0_attn_norm_w, L0_attn_skip_w, L0_attn_in_w, L0_attn_conv_w, L0_attn_conv_b, L0_attn_wd1, L0_attn_wd2, L0_attn_wd2_b, L0_attn_wB, L0_attn_wC, L0_attn_A_log, L0_attn_W_D, L0_attn_out_w), axis=-1)
    x = _layernorm(x + _L0_xattn_ref(16, 256, 512, L0_xattn_time_decay, L0_xattn_time_first, x, ctx_2048), axis=-1)
    x = _layernorm(x + _L0_ffn_ref(x, L0_ffn_wq_gate, L0_ffn_s_gate, L0_ffn_wq_up, L0_ffn_s_up, L0_ffn_wq_down, L0_ffn_s_down), axis=-1)
    return x

_drawn_inputs = setup_inputs


def setup_inputs(seed=0):
    import zlib

    import numpy as np

    out = dict(_drawn_inputs(seed))
    spreads = {'L0_attn_norm_w': (1.0, 0.6), 'L0_attn_conv_b': (0.0, 0.8), 'L0_attn_W_D': (1.0, 0.6)}
    factors = {'L0_attn_skip_w': 7.055,
     'L0_attn_in_w': 7.234,
     'L0_attn_conv_w': 7.354,
     'L0_attn_wd1': 8.0,
     'L0_attn_wd2': 8.0,
     'L0_attn_wd2_b': 8.0,
     'L0_attn_wB': 8.0,
     'L0_attn_wC': 8.0,
     'L0_attn_A_log': 8.0,
     'L0_attn_out_w': 6.412,
     'L0_ffn_s_gate': 5.909,
     'L0_ffn_s_up': 6.621,
     'L0_ffn_s_down': 3.012}
    for name, (base, spread) in spreads.items():
        noise = np.random.default_rng([zlib.crc32(name.encode()), seed]).standard_normal(out[name].shape)
        drawn = base * np.exp(spread * noise) if base else spread * noise
        out[name] = jnp.asarray(drawn.astype(out[name].dtype))
    for name, factor in factors.items():
        out[name] = (out[name] * factor).astype(out[name].dtype)
    return out
```

```python
import concourse.bass as bass
from concourse import mybir
from contextlib import ExitStack

FP32 = mybir.dt.float32
INT32 = mybir.dt.int32
ALU = mybir.AluOpType
ACT = mybir.ActivationFunctionType

P = 128
B, L, D = 16, 256, 512
E, N, R, K = 1024, 16, 128, 4
HID = 1408
DC, EC, HC = D // P, E // P, HID // P
QN, QC = 4, 2
UNITS = QN * N
EPS = 1e-5
DOWN = 64
LN_2 = 0.6931471805599453
SMALL = 2.0 ** -10
ZERO_POINT = 128.0
NEG = -1e38
EXP_LN = "natural_log_exp_and_others"


def at(b, per, k=0):
    return b * per + (k + 1)


def due(value):
    return not isinstance(value, int) or value > 0


JOBS = [("dl", 1, QC, "B"), ("rms", 0, 1, "A"), ("out", 0, 2 * EC, "C"), ("mean", 0, 1, "T"),
        ("in", 0, 2 * DC, "A"), ("dl", 2, QC, "B"), ("in", 1, 2 * DC, "A"), ("var", 0, 1, "T"),
        ("in", 2, 2 * DC, "A"), ("in", 3, 2 * DC, "A"), ("dl", 3, QC, "B"), ("sk", 0, 2 * DC, "A"),
        ("sk", 1, 2 * DC, "A"), ("proj", 0, 2 * EC, "A"), ("sk", 2, 2 * DC, "A"), ("dl", 0, QC, "A"),
        ("sk", 3, 2 * DC, "A"), ("out", 1, 2 * EC, "C")]
BANKS = 3
BANK = {(name, idx): j % BANKS for j, (name, idx, _, _) in enumerate(JOBS)}
BY_DVE, BY_ACT, CHAIN_DVE, CHAIN_POOL = 5, 6, 8, 12
SUM_A, SUM_R, SUM_T, CONV_POOL, REFINE = 3, 11, 12, 8, 6
LEAVE_LAST, LEAVE, GATE = 4, 3, 8
CONV_DVE, SOFT_DVE, SOFT_POOL, SILU_X = 8, 8, 15, 12
TOTAL = sum(n for _, _, n, _ in JOBS)
PER = {"rms": 1, "dl": QN, "mean": 1, "out": 2, "var": 1, "in": 4, "sk": 4, "proj": 1}
AHEAD = {"A": 1, "B": 0, "C": -1, "T": -2}


def plan():
    pieces, end, done = [[] for _ in range(UNITS)], {}, 0
    for j, (name, idx, n, _) in enumerate(JOBS):
        m = 0
        while m < n:
            slot = (done + m) * UNITS // TOTAL
            m1 = m
            while m1 < n and (done + m1) * UNITS // TOTAL == slot:
                m1 += 1
            pieces[slot].append((j, m, m1))
            m = m1
        done += n
        end[name, idx] = slot
    return pieces, end


PIECES, END = plan()


def stages(i):
    if i is None:
        return "ABCT"
    return "".join(s for s in "ABCT" if 0 <= i + AHEAD[s] < B)


def before_in_bank(j, now, earlier):
    for k in range(j - BANKS, -1, -BANKS):
        if JOBS[k][3] in now:
            return k, 0
    for k in range(len(JOBS) - BANKS + j % BANKS, -1, -BANKS):
        if JOBS[k][3] in earlier:
            return k, 1
    return None


def pass1(nc, x_t, w, x1_d, bc_d):
    with ExitStack() as ctx:
        def sb(name, shape, dt=FP32):
            return ctx.enter_context(nc.sbuf_tensor(name, shape, dt))

        def sem(name):
            return ctx.enter_context(nc.semaphore(name))

        in_w = sb("in_w", [P, DC, E])
        skip_w = sb("skip_w", [P, DC, E])
        wd1 = sb("wd1", [P, EC, R])
        wbc = sb("wbc", [P, EC, 2 * N])
        wd2 = sb("wd2", [P, E])
        out_w = sb("out_w", [P, EC, D])
        norm_w = sb("norm_w", [P, DC])
        conv_w = sb("conv_w", [P, EC, K])
        conv_b = sb("conv_b", [P, EC])
        wd2_b = sb("wd2_b", [P, EC])
        w_d = sb("w_d", [P, EC])
        neg_a = sb("neg_a", [P, EC, N])
        ident = sb("ident", [P, P])
        over_d = sb("over_d", [P, P])
        eps = sb("eps", [P, 2])
        xa = sb("xa", [P, DC, L])
        xr = [sb(f"xr{m}", [P, DC, L]) for m in range(2)]
        rn = sb("rn", [P, DC, L])
        xpad = sb("xpad", [P, 2, K - 1 + L])
        taps = sb("taps", [P, K - 1, L])
        xc = [sb(f"xc{m}", [P, EC, L]) for m in range(2)]
        gate = [sb(f"gate{m}", [P, EC, L]) for m in range(2)]
        yg = [sb(f"yg{m}", [P, EC, L]) for m in range(2)]
        d1 = sb("d1", [P, L])
        bc = sb("bc", [2 * N, L])
        bcs = sb("bcs", [P, N, 2, L])
        v_sb = sb("v_sb", [P, QC, L])
        e_sb = sb("e_sb", [P, QC, L])
        z_sb = sb("z_sb", [P, QC, L])
        l_sb = sb("l_sb", [P, QC, L])
        r_sb = sb("r_sb", [P, QC, L])
        p_sb = sb("p_sb", [P, QC, L])
        small = sb("small", [P, 3])
        delta = sb("delta", [P, 2, QC, L])
        dx = sb("dx", [P, 2, QC, L])
        u = sb("u", [P, 4, QC, L])
        hc = sb("hc", [P, 4, QC, L])
        sq = sb("sq", [P, DC, L])
        ln_a = sb("ln_a", [P, L])
        rstd_a = sb("rstd_a", [P, 1, L])
        ln_t = sb("ln_t", [P, L])
        rstd_t = sb("rstd_t", [P, 1, L])
        a_ps = [ctx.enter_context(nc.psum_tensor(f"a_ps{m}", [P, QC, L], FP32)) for m in range(2)]
        h_ps = [ctx.enter_context(nc.psum_tensor(f"h_ps{m}", [P, QC, L], FP32)) for m in range(2)]
        y_ps = ctx.enter_context(nc.psum_tensor("y_ps", [P, QC, L], FP32))
        job_ps = [ctx.enter_context(nc.psum_tensor(f"job_ps{m}", [P, QC, L], FP32)) for m in range(BANKS)]

        names = ("weights zero_id const neg_exp neg_ready norm_folded xa_in xr_in sqa ln_a rstd_a "
                 "rms_read half_r refined rn conv_dve conv_pool "
                 "in_read silu_x sk_read silu_g d1_read bc_read v_read e_exp z ln1p small_e rounded square lost s1 delta dx "
                 "ln_small sum_a sum_r sum_t a u scan hc nsum y_read yg r center sqt ln_t rstd_t x1 x1_stored bc_stored").split()
        s = {n: sem("s_" + n) for n in names}
        full = {n: sem("s_full_" + n) for n in PER}
        s_bc = [sem(f"s_bc_in{g}") for g in range(4)]
        freed = {"rms": (s["rms_read"], 1, 1), "dl": (s["v_read"], QN * QC, QC), "mean": (s["center"], 1, 1), "out": (s["r"], 2, 1),
                 "var": (s["ln_t"], 1, 1), "in": (s["in_read"], 4, 1), "sk": (s["sk_read"], 4, 1), "proj": (s["bc_read"], 1, 1)}
        block = ctx.enter_context(nc.Block())

        def steps(eng, step):
            for i in (-1, 0, 1, 2):
                step(i, i % 2, stages(i), stages(i - 1))
            with eng.Fori(0, 5) as j:
                for m in (1, 0):
                    step(j * 2 + (4 - m), m, stages(None), stages(None))
            for i in (13, 14, 15, 16, 17):
                step(i, i % 2, stages(i), stages(i - 1))

        @block.sync
        def _(sp):
            for dst, src in ((in_w, w["in_w"]), (skip_w, w["skip_w"]), (wd1, w["wd1"]), (wbc, w["wbc"]), (wd2, w["wd2"]),
                             (out_w, w["out_w"]), (norm_w, w["norm_w"]), (conv_w, w["conv_w"]), (conv_b, w["conv_b"]),
                             (wd2_b, w["wd2_b"]), (w_d, w["w_d"]), (neg_a, w["a_log"])):
                sp.dma_start(dst[:], src).then_inc(s["weights"], 16)
            sp.dma_start(xa[:], x_t[0]).then_inc(s["xa_in"], 16)

            def step(i, m, now, _):
                if "A" in now and not (isinstance(i, int) and i + 2 >= B):
                    sp.wait_ge(s["rn"], at(i + 1, 1))
                    sp.dma_start(xa[:], x_t[i + 2]).then_inc(s["xa_in"], 16)
                if "T" in now:
                    sp.wait_ge(s["x1"], at(i - 2, 1))
                    sp.dma_start(x1_d[i - 2], xr[m][:]).then_inc(s["x1_stored"], 16)
                if "B" in now:
                    if not (isinstance(i, int) and i < 2):
                        sp.wait_ge(s["x1_stored"], at(i - 2, 16, 15))
                    sp.dma_start(xr[m][:], x_t[i]).then_inc(s["xr_in"], 16)
                if "A" in now:
                    sp.wait_ge(s["bc_read"], at(i + 1, 1))
                    for t in range(2):
                        sp.dma_start(bc_d[i + 1, :, t], bc[t * N:(t + 1) * N, :]).then_inc(s["bc_stored"], 16)
                    sp.wait_ge(s["bc_stored"], at(i + 1, 32, 31))
                    for g in range(4):
                        if "B" in now:
                            sp.wait_ge(s["u"], at(i, UNITS, 3 * N + 4 * g + 3))
                            sp.wait_ge(s["hc"], at(i, UNITS, 3 * N + 4 * g + 3))
                        sp.dma_start(bcs[:, 4 * g:4 * g + 4],
                                     bc_d[i + 1, 4 * g:4 * g + 4].partition_broadcast(P)).then_inc(s_bc[g], 16)
            steps(sp, step)
            sp.wait_ge(s["x1_stored"], 16 * B)

        @block.scalar
        def _(act):
            act.preload_act_table_set(EXP_LN)
            act.wait_ge(s["weights"], 16 * 12)
            nc.scalar.activation(neg_a[:], neg_a[:], ACT.Exp).then_inc(s["neg_exp"], 1)
            act.wait_ge(s["norm_folded"], 1)
            nc.scalar.activation(small[:, 2:3], small[:, 2:3], ACT.Ln, bias=small[:, 1:2]).then_inc(s["ln_small"], 1)

            def exp_unit(i, m, k):
                q, n = divmod(k, N)
                if n == 0:
                    act.wait_ge(s["delta"], at(i, QN, q))
                if due(at(i, UNITS, k - 2)):
                    act.wait_ge(s["scan"], at(i, UNITS, k - 2))
                for c in range(QC):
                    ins = nc.scalar.activation(a_ps[k % 2][:, c, 1:L], delta[:, q % 2, c, 1:L], ACT.Exp,
                                               scale=neg_a[:, QC * q + c, n:n + 1])
                ins.then_inc(s["a"], 1)

            def softplus(b, q, part):
                if part < QC:
                    if part == 0:
                        act.wait_ge(full["dl"], at(b, QN, q))
                        if due(at(b, QN, q - 1)):
                            act.wait_ge(s["delta"], at(b, QN, q - 1))
                    src = job_ps[BANK["dl", q]][:, part]
                    bias = wd2_b[:, QC * q + part:QC * q + part + 1]
                    nc.scalar.activation(v_sb[:, part], src, ACT.Relu, bias=bias)
                    nc.scalar.activation(e_sb[:, part], src, ACT.Abs, bias=bias).then_inc(s["v_read"], 1)
                elif part == QC:
                    act.wait_ge(s["v_read"], at(b, QN * QC, QC * q + QC - 1))
                    nc.scalar.activation(e_sb[:], e_sb[:], ACT.Exp, scale=-1.0).then_inc(s["e_exp"], 1)
                elif part == QC + 1:
                    act.wait_ge(s["e_exp"], at(b, QN, q))
                    nc.scalar.activation(z_sb[:], e_sb[:], ACT.Relu, bias=small[:, 0:1]).then_inc(s["z"], 1)
                else:
                    act.wait_ge(s["z"], at(b, QN, q))
                    nc.scalar.activation(l_sb[:], z_sb[:], ACT.Ln, bias=small[:, 1:2]).then_inc(s["ln1p"], 1)

            def leave_in(b, m, p, part):
                bank = job_ps[BANK["in", p]]
                odd = QC * p + 1
                if part == 0:
                    act.wait_ge(full["in"], at(b, 4, p))
                    if due(at(b * 4 + p - 2, 3, 2)):
                        act.wait_ge(s["conv_dve"], at(b * 4 + p - 2, 3, 2))
                    if due(at(b * 4 + p - 1, 3, 2)):
                        act.wait_ge(s["conv_pool"], at(b * 4 + p - 1, 3, 2))
                    nc.scalar.activation(xpad[:, p % 2, K - 1:], bank[:, 0], ACT.Identity)
                if part < 2:
                    for tap in ((2,), (1, 0))[part]:
                        lag = K - 1 - tap
                        nc.scalar.activation(taps[:, tap, lag:], bank[:, 1, 0:L - lag], ACT.Identity,
                                             scale=conv_w[:, odd, tap:tap + 1])
                    return
                if p == 0:
                    if due(at(b - 2, QN, 3)):
                        act.wait_ge(s["y_read"], at(b - 2, QN, 3))
                for c in range(QC):
                    ch = QC * p + c
                    ins = nc.scalar.activation(xc[m][:, ch], bank[:, c], ACT.Identity,
                                               bias=conv_b[:, ch:ch + 1], scale=conv_w[:, ch, K - 1:K])
                ins.then_inc(s["in_read"], 1)

            def rstd(b, job, ln, out, s_ln, s_out, s_used):
                act.wait_ge(full[job], at(b, 1))
                if due(at(b - 1, 1)):
                    act.wait_ge(s_used, at(b - 1, 1))
                nc.scalar.activation(ln[:], job_ps[BANK[job, 0]][:, 0], ACT.Ln, bias=eps[:, 0:1],
                                     scale=2.0 ** -DOWN).then_inc(s_ln, 1)
                act.wait_ge(s_ln, at(b, 1))
                nc.scalar.activation(out[:, 0], ln[:], ACT.Exp, bias=eps[:, 1:2],
                                     scale=-0.5).then_inc(s_out, 1)

            def step(i, m, now, _):
                nm = 1 - m
                for k in range(UNITS):
                    if "B" in now:
                        exp_unit(i, m, k)
                    if "T" in now and k == END["mean", 0] + BY_DVE + 3:
                        act.wait_ge(s["center"], at(i - 2, 1))
                        act.wait_ge(full["mean"], at(i - 2, 1))
                        nc.scalar.activation(sq[:], xr[m][:], ACT.Square).then_inc(s["sqt"], 1)
                    if "T" in now and k == END["var", 0] + BY_ACT:
                        rstd(i - 2, "var", ln_t, rstd_t, s["ln_t"], s["rstd_t"], s["x1"])
                    for q in (1, 2, 3):
                        if "B" in now and 0 <= k - END["dl", q] - BY_ACT < QC + 3:
                            softplus(i, q, k - END["dl", q] - BY_ACT)
                    if "A" not in now:
                        continue
                    b = i + 1
                    if k == 0:
                        act.wait_ge(s["xa_in"], at(b, 16, 15))
                        if due(at(b - 1, 4, 3)):
                            act.wait_ge(full["sk"], at(b - 1, 4, 3))
                        nc.scalar.activation(rn[:], xa[:], ACT.Square).then_inc(s["sqa"], 1)
                    if k == END["rms", 0] + BY_ACT:
                        rstd(b, "rms", ln_a, rstd_a, s["ln_a"], s["rstd_a"], s["rn"])
                    for p in range(4):
                        part = k - END["in", p] - BY_ACT
                        if 0 <= part < 3:
                            leave_in(b, nm, p, part)
                        if k == END["sk", p] + BY_ACT:
                            act.wait_ge(full["sk"], at(b, 4, p))
                            if p == 0:
                                if due(at(b - 2, QN, 3)):
                                    act.wait_ge(s["yg"], at(b - 2, QN, 3))
                            nc.scalar.activation(gate[nm][:, QC * p:QC * p + QC], job_ps[BANK["sk", p]][:],
                                                 ACT.Identity).then_inc(s["sk_read"], 1)
                    if k == END["in", 3] + SILU_X:
                        act.wait_ge(s["conv_dve"], at(b * 4 + 3, 3, 2))
                        act.wait_ge(s["conv_pool"], at(b * 4 + 3, 3, 2))
                        nc.scalar.activation(xc[nm][:], xc[nm][:], ACT.Silu).then_inc(s["silu_x"], 1)
                        act.preload_act_table_set(EXP_LN)
                    if k == END["sk", 3] + BY_ACT + 1:
                        act.wait_ge(s["sk_read"], at(b, 4, 3))
                        nc.scalar.activation(gate[nm][:], gate[nm][:], ACT.Silu).then_inc(s["silu_g"], 1)
                        act.preload_act_table_set(EXP_LN)
                    if k == END["proj", 0] + BY_ACT:
                        act.wait_ge(full["proj"], at(b, 1))
                        if due(at(b - 1, QN, 3)):
                            act.wait_ge(full["dl"], at(b - 1, QN, 3))
                        nc.scalar.activation(d1[:], job_ps[BANK["proj", 0]][:, 0], ACT.Identity).then_inc(s["d1_read"], 1)
                        if due(at(b - 1, 32, 31)):
                            act.wait_ge(s["bc_stored"], at(b - 1, 32, 31))
                        nc.scalar.activation(bc[:], job_ps[BANK["proj", 0]][0:2 * N, 1], ACT.Identity).then_inc(s["bc_read"], 1)
                    if 0 <= k - END["dl", 0] - BY_ACT < QC + 3:
                        softplus(b, 0, k - END["dl", 0] - BY_ACT)
            steps(act, step)

        @block.vector
        def _(dve):
            dve.wait_ge(s["neg_exp"], 1)
            nc.vector.tensor_scalar(neg_a[:], neg_a[:], -1.0, None, ALU.mult).then_inc(s["neg_ready"], 1)
            nc.vector.memset(over_d[:], 1.0 / D)
            nc.vector.memset(eps[:, 0:1], EPS * 2.0 ** -DOWN)
            nc.vector.memset(eps[:, 1:2], -0.5 * DOWN * LN_2)
            for n, value in enumerate((-SMALL, 1.0 + SMALL, 0.0)):
                nc.vector.memset(small[:, n:n + 1], value)
            nc.vector.memset(xpad[:, :, 0:K - 1], 0.0)
            nc.vector.memset(taps[:, :, 0:K - 1], 0.0)
            for m in range(2):
                nc.vector.memset(a_ps[m][:, :, 0:1], 0.0)
            for wt in (in_w, skip_w):
                for c in range(DC):
                    ins = nc.vector.tensor_scalar(wt[:, c], wt[:, c], norm_w[:, c:c + 1], None, ALU.mult)
            ins.then_inc(s["norm_folded"], 1)
            dve.wait_ge(s["norm_folded"], 1)
            dve.wait_ge(s["ln_small"], 1)

            def scan_unit(i, k):
                dve.wait_ge(s["a"], at(i, UNITS, k))
                dve.wait_ge(s["u"], at(i, UNITS, k))
                if due(at(i, UNITS, k - 2)):
                    dve.wait_ge(s["hc"], at(i, UNITS, k - 2))
                nc.vector.tensor_tensor_scan(h_ps[k % 2][:].rearrange("p c t -> p (c t)"),
                                             a_ps[k % 2][:].rearrange("p c t -> p (c t)"),
                                             u[:, k % 4].rearrange("p c t -> p (c t)"),
                                             0.0, ALU.mult, ALU.add).then_inc(s["scan"], 1)

            def times_c(i, k):
                q, n = divmod(k, N)
                if q == 0 and n % 4 == 0:
                    dve.wait_ge(s_bc[n // 4], at(i, 16, 15))
                dve.wait_ge(s["scan"], at(i, UNITS, k))
                if due(at(i, UNITS, k - 4)):
                    dve.wait_ge(s["nsum"], at(i, UNITS, k - 4))
                nc.vector.tensor_tensor(hc[:, k % 4], h_ps[k % 2][:],
                                        bcs[:, n, 1:2].to_broadcast([P, QC, L]), ALU.mult).then_inc(s["hc"], 1)

            def leave_y(b, m, q):
                dve.wait_ge(s["nsum"], at(b, UNITS, N * q + N - 1))
                if q == 0:
                    if due(at(b - 2, 2, 1)):
                        dve.wait_ge(full["out"], at(b - 2, 2, 1))
                for c in range(QC):
                    ch = QC * q + c
                    ins = nc.vector.scalar_tensor_tensor(yg[m][:, ch], xc[m][:, ch], w_d[:, ch:ch + 1],
                                                         y_ps[:, c], ALU.mult, ALU.add)
                ins.then_inc(s["y_read"], 1)

            def conv(b, m, p, t):
                ch, tap = QC * p, K - 2 - t
                if t:
                    dve.wait_ge(s["conv_dve"], at(b * 4 + p, 3, t - 1))
                else:
                    dve.wait_ge(s["in_read"], at(b, 4, p))
                nc.vector.scalar_tensor_tensor(xc[m][:, ch], xpad[:, p % 2, tap:tap + L],
                                               conv_w[:, ch, tap:tap + 1], xc[m][:, ch],
                                               ALU.mult, ALU.add).then_inc(s["conv_dve"], 1)

            def softplus(b, q, part):
                if part == 0:
                    dve.wait_ge(s["e_exp"], at(b, QN, q))
                    nc.vector.tensor_scalar(p_sb[:], e_sb[:], SMALL, None, ALU.min).then_inc(s["small_e"], 1)
                    dve.wait_ge(s["z"], at(b, QN, q))
                    nc.vector.tensor_scalar(r_sb[:], z_sb[:], 1.0 + SMALL, -1.0 - SMALL,
                                            ALU.add, ALU.add).then_inc(s["rounded"], 1)
                elif part == 1:
                    dve.wait_ge(s["small_e"], at(b, QN, q))
                    nc.vector.scalar_tensor_tensor(p_sb[:], p_sb[:], -2.0, p_sb[:],
                                                   ALU.add, ALU.mult).then_inc(s["square"], 1)
                elif part == 2:
                    dve.wait_ge(s["rounded"], at(b, QN, q))
                    nc.vector.scalar_tensor_tensor(r_sb[:], r_sb[:], -1.0, z_sb[:],
                                                   ALU.mult, ALU.add).then_inc(s["lost"], 1)
                else:
                    dve.wait_ge(s["ln1p"], at(b, QN, q))
                    nc.vector.scalar_tensor_tensor(v_sb[:], l_sb[:], small[:, 2:3], v_sb[:],
                                                   ALU.subtract, ALU.add)
                    dve.wait_ge(s["square"], at(b, QN, q))
                    dve.wait_ge(s["lost"], at(b, QN, q))
                    nc.vector.scalar_tensor_tensor(p_sb[:], p_sb[:], -0.5, r_sb[:],
                                                   ALU.mult, ALU.add).then_inc(s["s1"], 1)

            def refine(b):
                dve.wait_ge(s["rstd_a"], at(b, 1))
                dve.wait_ge(full["rms"], at(b, 1))
                r = rstd_a[:, 0]
                nc.vector.scalar_tensor_tensor(ln_a[:], job_ps[BANK["rms", 0]][:, 0], EPS, r,
                                               ALU.add, ALU.mult).then_inc(s["rms_read"], 1)
                dve.wait_ge(s["rms_read"], at(b, 1))
                nc.vector.scalar_tensor_tensor(ln_a[:], ln_a[:], -0.5, r, ALU.mult, ALU.mult).then_inc(s["half_r"], 1)
                dve.wait_ge(s["half_r"], at(b, 1))
                nc.vector.scalar_tensor_tensor(r, ln_a[:], 1.5, r, ALU.add, ALU.mult).then_inc(s["refined"], 1)

            def residual(b, m, j):
                bank = BANK["out", j]
                if j == 0:
                    dve.wait_ge(s["xr_in"], at(b, 16, 15))
                dve.wait_ge(full["out"], at(b, 2, j))
                part = xr[m][:, 2 * j:2 * j + 2]
                nc.vector.scalar_tensor_tensor(part, part, 2.0, job_ps[bank][:], ALU.mult, ALU.add).then_inc(s["r"], 1)

            def step(i, m, now, _):
                nm = 1 - m
                for k in range(UNITS):
                    if "B" in now:
                        scan_unit(i, k)
                        if k:
                            times_c(i, k - 1)
                    if "T" in now and k == END["out", 1] + BY_DVE - UNITS:
                        residual(i - 2, m, 1)
                    if "T" in now and k == END["mean", 0] + BY_DVE:
                        dve.wait_ge(full["mean"], at(i - 2, 1))
                        dve.wait_ge(s["r"], at(i - 2, 2, 1))
                        dve.wait_ge(s["sum_r"], at(i - 2, 2, 0))
                        nc.vector.tensor_tensor(xr[m][:], xr[m][:], job_ps[BANK["mean", 0]][:, 0:1].to_broadcast([P, DC, L]),
                                                ALU.subtract).then_inc(s["center"], 1)
                    if "T" in now and k == END["var", 0] + CHAIN_DVE:
                        dve.wait_ge(s["rstd_t"], at(i - 2, 1))
                        dve.wait_ge(s["center"], at(i - 2, 1))
                        nc.vector.tensor_tensor(xr[m][:], xr[m][:], rstd_t[:].to_broadcast([P, DC, L]),
                                                ALU.mult).then_inc(s["x1"], 1)
                    if "C" in now and k == LEAVE_LAST:
                        leave_y(i - 1, nm, 3)
                    if "C" in now and k == END["out", 0] + BY_DVE:
                        residual(i - 1, nm, 0)
                    if "B" in now:
                        for q in range(3):
                            if k == N * (q + 1) + LEAVE:
                                leave_y(i, m, q)
                        for q in (1, 2, 3):
                            if 0 <= k - END["dl", q] - SOFT_DVE < 4:
                                softplus(i, q, k - END["dl", q] - SOFT_DVE)
                    if "A" in now:
                        if k == END["rms", 0] + REFINE:
                            refine(i + 1)
                        for p in range(4):
                            if 0 <= k - END["in", p] - CONV_DVE < 3:
                                conv(i + 1, nm, p, k - END["in", p] - CONV_DVE)
                        if 0 <= k - END["dl", 0] - SOFT_DVE < 4:
                            softplus(i + 1, 0, k - END["dl", 0] - SOFT_DVE)
                if "B" in now:
                    times_c(i, UNITS - 1)
            steps(dve, step)

        @block.gpsimd
        def _(pool):
            nc.gpsimd.memset(ident[:], 0.0).then_inc(s["zero_id"], 1)
            pool.wait_ge(s["zero_id"], 1)
            nc.gpsimd.affine_select(out=ident[:], in_=ident[:], compare_op=ALU.not_equal, fill=1.0, base=0,
                                    pattern=[[-1, P]], channel_multiplier=1).then_inc(s["const"], 1)

            def times_b(i, k):
                q, n = divmod(k, N)
                if n == 0:
                    pool.wait_ge(s["dx"], at(i, QN, q))
                if q == 0 and n % 4 == 0:
                    pool.wait_ge(s_bc[n // 4], at(i, 16, 15))
                if due(at(i, UNITS, k - 4)):
                    pool.wait_ge(s["scan"], at(i, UNITS, k - 4))
                nc.gpsimd.tensor_tensor(u[:, k % 4], dx[:, q % 2], bcs[:, n, 0:1].to_broadcast([P, QC, L]),
                                        ALU.mult).then_inc(s["u"], 1)

            def delta_dx(b, m, q):
                pool.wait_ge(s["s1"], at(b, QN, q))
                if due(at(b * QN + q - 2, N, N - 1)):
                    pool.wait_ge(s["a"], at(b * QN + q - 2, N, N - 1))
                nc.gpsimd.tensor_tensor(delta[:, q % 2], v_sb[:], p_sb[:], ALU.add).then_inc(s["delta"], 1)
                pool.wait_ge(s["delta"], at(b, QN, q))
                if due(at(b * QN + q - 2, N, N - 1)):
                    pool.wait_ge(s["u"], at(b * QN + q - 2, N, N - 1))
                if q == 0:
                    pool.wait_ge(s["silu_x"], at(b, 1))
                nc.gpsimd.tensor_tensor(dx[:, q % 2], delta[:, q % 2], xc[m][:, QC * q:QC * q + QC],
                                        ALU.mult).then_inc(s["dx"], 1)

            def halve(out, src, s_out):
                nc.gpsimd.tensor_tensor(out[:, 0:2], src[:, 0:2], src[:, 2:4], ALU.add).then_inc(s_out, 1)

            def total(out, s_out):
                nc.gpsimd.tensor_tensor(out[:, 0], out[:, 0], out[:, 1], ALU.add).then_inc(s_out, 1)

            def conv(b, m, p, t):
                ch, tap = QC * p + 1, K - 2 - t
                if t:
                    pool.wait_ge(s["conv_pool"], at(b * 4 + p, 3, t - 1))
                else:
                    pool.wait_ge(s["in_read"], at(b, 4, p))
                nc.gpsimd.tensor_tensor(xc[m][:, ch], xc[m][:, ch], taps[:, tap],
                                        ALU.add).then_inc(s["conv_pool"], 1)

            def gated(b, m, q):
                pool.wait_ge(s["y_read"], at(b, QN, q))
                if q == 0:
                    pool.wait_ge(s["silu_g"], at(b, 1))
                part = yg[m][:, QC * q:QC * q + QC]
                nc.gpsimd.tensor_tensor(part, part, gate[m][:, QC * q:QC * q + QC],
                                        ALU.mult).then_inc(s["yg"], 1)

            def step(i, m, now, _):
                nm = 1 - m
                for k in range(UNITS):
                    if "B" in now:
                        times_b(i, k)
                    if "C" in now and k == GATE:
                        gated(i - 1, nm, 3)
                    if "T" in now and k == SUM_R:
                        if due(at(i - 3, 1)):
                            pool.wait_ge(full["var"], at(i - 3, 1))
                        pool.wait_ge(s["r"], at(i - 2, 2, 1))
                        halve(sq, xr[m], s["sum_r"])
                        pool.wait_ge(s["sum_r"], at(i - 2, 2, 0))
                        total(sq, s["sum_r"])
                    if "T" in now and k == END["mean", 0] + SUM_T:
                        pool.wait_ge(s["sqt"], at(i - 2, 1))
                        halve(sq, sq, s["sum_t"])
                        pool.wait_ge(s["sum_t"], at(i - 2, 2, 0))
                        total(sq, s["sum_t"])
                    if "A" in now and k == SUM_A:
                        pool.wait_ge(s["sqa"], at(i + 1, 1))
                        halve(rn, rn, s["sum_a"])
                        pool.wait_ge(s["sum_a"], at(i + 1, 2, 0))
                        total(rn, s["sum_a"])
                    if "A" in now and k == END["rms", 0] + CHAIN_POOL - 2:
                        pool.wait_ge(s["refined"], at(i + 1, 1))
                        nc.gpsimd.tensor_tensor(rn[:], xa[:], rstd_a[:].to_broadcast([P, DC, L]),
                                                ALU.mult).then_inc(s["rn"], 1)
                    if "B" in now:
                        for q in range(3):
                            if k == N * (q + 1) + GATE:
                                gated(i, m, q)
                        for q in (1, 2, 3):
                            if k == END["dl", q] + SOFT_POOL:
                                delta_dx(i, m, q)
                    if "A" in now:
                        for p in range(4):
                            if 0 <= k - END["in", p] - CONV_POOL < 3:
                                conv(i + 1, nm, p, k - END["in", p] - CONV_POOL)
                    if "A" in now and k == min(END["dl", 0] + SOFT_POOL, UNITS - 1):
                        delta_dx(i + 1, nm, 0)
            steps(pool, step)

        @block.tensor
        def _(pe):
            pe.wait_ge(s["weights"], 16 * 12)
            pe.wait_ge(s["const"], 1)
            pe.wait_ge(s["norm_folded"], 1)

            def mm(out, lhs, rhs, k, n):
                return nc.tensor.matmul(out, lhs, rhs, start=(k == 0), stop=(k == n - 1))

            def job_matmul(job, idx, bank, m, x):
                if job in ("in", "sk"):
                    c, k = divmod(x, DC)
                    ch = (QC * idx + c) * P
                    wt = in_w if job == "in" else skip_w
                    return mm(bank[:, c], wt[:, k, ch:ch + P], rn[:, k], k, DC)
                if job in ("rms", "mean", "var"):
                    return mm(bank[:, 0], over_d[:], (rn if job == "rms" else sq)[:, 0], 0, 1)
                if job == "dl":
                    ch = (QC * idx + x) * P
                    return mm(bank[:, x], wd2[:, ch:ch + P], d1[:], 0, 1)
                if job == "proj":
                    c, k = divmod(x, EC)
                    if c == 0:
                        return mm(bank[:, 0], wd1[:, k], xc[1 - m][:, k], k, EC)
                    return mm(bank[0:2 * N, 1], wbc[:, k], xc[1 - m][:, k], k, EC)
                c, k = divmod(x, EC)
                ch = (2 * idx + c) * P
                return mm(bank[:, c], out_w[:, k, ch:ch + P], yg[1 - m][:, k], k, EC)

            def inputs(job, idx, b):
                if job == "rms":
                    pe.wait_ge(s["sum_a"], at(b, 2, 1))
                elif job in ("in", "sk"):
                    pe.wait_ge(s["rn"], at(b, 1))
                elif job == "mean":
                    pe.wait_ge(s["sum_r"], at(b, 2, 1))
                elif job == "var":
                    pe.wait_ge(s["sum_t"], at(b, 2, 1))
                elif job == "dl":
                    pe.wait_ge(s["d1_read"], at(b, 1))
                elif job == "proj":
                    pe.wait_ge(s["silu_x"], at(b, 1))
                else:
                    pe.wait_ge(s["yg"], at(b, QN, 3))

            def piece(i, m, now, earlier, j, lo, hi):
                job, idx, n, stage = JOBS[j]
                if stage not in now:
                    return
                b = i + AHEAD[stage]
                if lo == 0:
                    inputs(job, idx, b)
                    last = before_in_bank(j, now, earlier)
                    if last is not None:
                        k, ago = last
                        was, widx, _, wstage = JOBS[k]
                        sem_read, per, each = freed[was]
                        pe.wait_ge(sem_read, at(i - ago + AHEAD[wstage], per, each * widx + each - 1))
                for x in range(lo, hi):
                    ins = job_matmul(job, idx, job_ps[j % BANKS], m, x)
                if hi == n:
                    ins.then_inc(full[job], 1)

            def pieces(i, m, now, earlier, k):
                for j, lo, hi in PIECES[k]:
                    piece(i, m, now, earlier, j, lo, hi)

            def step(i, m, now, earlier):
                for k in range(UNITS):
                    q, n = divmod(k, N)
                    if n == 0:
                        pieces(i, m, now, earlier, k)
                    if "B" in now:
                        if n == 0:
                            if due(at(i, QN, q - 1)):
                                pe.wait_ge(s["y_read"], at(i, QN, q - 1))
                        pe.wait_ge(s["hc"], at(i, UNITS, k))
                        nc.tensor.matmul(y_ps[:], ident[:], hc[:, k % 4],
                                         start=(n == 0), stop=(n == N - 1)).then_inc(s["nsum"], 1)
                    if n:
                        pieces(i, m, now, earlier, k)
            steps(pe, step)


def pass2(nc, x1_d, ctx_t, w, out):
    GU = 4
    J_MEAN3, J_CENTER3, J_SQ3, J_VAR3 = 3, 3, 4, 6
    J_MEAN2, J_CENTER2, J_SQ2 = 7, 7, 8
    PARTS = {0: (5, 6), 1: (7,), 2: (8,), 4: (9,), J_CENTER2: (10,)}
    with ExitStack() as ctx:
        def sb(name, shape, dt=FP32):
            return ctx.enter_context(nc.sbuf_tensor(name, shape, dt))

        def pb(name, shape):
            return ctx.enter_context(nc.psum_tensor(name, shape, FP32))

        gate_w = sb("gate_w", [P, DC, HID])
        up_w = sb("up_w", [P, DC, HID])
        down_w = sb("down_w", [P, HC, D])
        s_gate = sb("s_gate", [P, HC])
        s_up = sb("s_up", [P, HC])
        s_down = sb("s_down", [P, DC])
        decay = sb("decay", [P, DC])
        decay_l = sb("decay_l", [P, DC, L])
        first = sb("first", [P, DC])
        over_d = sb("over_d2", [P, P])
        eps = sb("eps2", [P, 2])
        k_sb = sb("k_sb", [P, DC, L])
        v_in = sb("v_in", [P, DC, L])
        pp = sb("pp", [P, DC, L + 1])
        q_sb = sb("q_sb", [P, DC, L])
        e1 = sb("e1", [P, DC, L])
        e1b = sb("e1b", [P, DC, L])
        e2b = sb("e2b", [P, DC, L])
        ev = sb("ev", [P, DC, L])
        aa = sb("aa", [P, DC, L + 1])
        bb = sb("bb", [P, DC, L + 1])
        x2 = [sb(f"x2_{m}", [P, DC, L]) for m in range(2)]
        g_sb = sb("g_sb", [P, GU, L])
        h_sb = sb("h_sb", [P, HC, L])
        sq3 = sb("sq3", [P, DC, L])
        sums = {n: sb("sums_" + n, [P, 3, L]) for n in ("r3", "sq3", "r2", "sq2")}
        ln2 = sb("ln2", [P, L])
        rstd2 = sb("rstd2", [P, 1, L])
        ln3 = sb("ln3", [P, L])
        rstd3 = sb("rstd3", [P, 1, L])
        gu_ps = [pb(f"gu_ps{j}", [P, 2, L]) for j in range(GU)]
        dn_ps = [pb(f"dn_ps{j}", [P, 2, L]) for j in range(2)]
        st2_ps = pb("st2_ps", [P, 2, L])
        st3_ps = pb("st3_ps", [P, 2, L])
        names = ("vectors in_gate in_up in_down converted dec_exp const k_in v_in pp q d1 d2 d3 d4 e1 e2 e1b e2b bb aa ev n1 n2 m1 den rec "
                 "num y r2 center2 sq2 ln2 rstd2 x2 gu silu h down r3 mean3 center3 sq3 var3 ln3 rstd3 x3 stored "
                 "mean2 var2 half_r3 sum_r3 half_sq3 sum_sq3 half_r2 sum_r2 half_sq2 sum_sq2").split()
        s = {n: ctx.enter_context(nc.semaphore("t_" + n)) for n in names}
        block = ctx.enter_context(nc.Block())
        N_V = 5

        def steps(eng, step):
            for i in (-1, 0, 1):
                step(i, i % 2, *present(i))
            with eng.Fori(0, 6) as j:
                for m in range(2):
                    step(j * 2 + (2 + m), m, True, True, True)
            for i in (14, 15, 16):
                step(i, i % 2, *present(i))

        def present(i):
            return 0 <= i + 1 < B, 0 <= i < B, 0 <= i - 1 < B

        def flat(t):
            return t.rearrange("p c t -> p (c t)")

        @block.sync
        def _(sp):
            for dst, src in ((decay, w["decay"]), (first, w["first"]), (s_gate, w["s_gate"]), (s_up, w["s_up"]),
                             (s_down, w["s_down"])):
                sp.dma_start(dst[:], src).then_inc(s["vectors"], 16)
            sp.dma_start(k_sb[:], x1_d[0]).then_inc(s["k_in"], 16)
            sp.dma_start(v_in[:], ctx_t[0]).then_inc(s["v_in"], 16)
            for name, dst in (("gate", gate_w), ("up", up_w), ("down", down_w)):
                sp.dma_start(dst[:].bitcast(INT32), w[name]).then_inc(s["in_" + name], 16)

            def step(i, m, W, F, Z):
                if Z:
                    sp.wait_ge(s["x3"], at(i - 1, 1))
                    sp.dma_start(out[i - 1], x2[1 - m][:]).then_inc(s["stored"], 16)
                if W and not (isinstance(i, int) and i + 2 >= B):
                    sp.wait_ge(s["n2"], at(i + 1, 1))
                    sp.dma_start(v_in[:], ctx_t[i + 2]).then_inc(s["v_in"], 16)
                    sp.wait_ge(s["r2"], at(i + 1, 1))
                    sp.dma_start(k_sb[:], x1_d[i + 2]).then_inc(s["k_in"], 16)
            steps(sp, step)
            sp.wait_ge(s["stored"], 16 * B)

        @block.scalar
        def _(act):
            act.preload_act_table_set(EXP_LN)
            act.wait_ge(s["vectors"], 16 * N_V)
            nc.scalar.activation(decay[:], decay[:], ACT.Exp).then_inc(s["dec_exp"], 1)
            act.wait_ge(s["const"], 1)

            def rstd(b, src, s_full, ln, to, s_ln, s_to, s_used):
                act.wait_ge(s_full, at(b, 1))
                if due(at(b - 1, 1)):
                    act.wait_ge(s_used, at(b - 1, 1))
                nc.scalar.activation(ln[:], src, ACT.Ln, bias=eps[:, 0:1],
                                     scale=2.0 ** -DOWN).then_inc(s_ln, 1)
                act.wait_ge(s_ln, at(b, 1))
                nc.scalar.activation(to[:, 0], ln[:], ACT.Exp, bias=eps[:, 1:2],
                                     scale=-0.5).then_inc(s_to, 1)

            def silu(b, j):
                act.wait_ge(s["gu"], at(b, HC, j))
                if due(at(b, HC, j - GU) if j >= GU else at(b - 1, HC, HC - 1)):
                    act.wait_ge(s["h"], at(b, HC, j - GU) if j >= GU else at(b - 1, HC, HC - 1))
                nc.scalar.activation(g_sb[:, j % GU], gu_ps[j % GU][:, 0], ACT.Silu,
                                     scale=s_gate[:, j:j + 1]).then_inc(s["silu"], 1)

            def exp(b, buf, s_d, s_e):
                act.wait_ge(s_d, at(b, 1))
                nc.scalar.activation(buf[:], buf[:], ACT.Exp).then_inc(s_e, 1)

            def step(i, m, W, F, Z):
                b = i + 1
                if W:
                    exp(b, e2b, s["d4"], s["e2b"])
                    exp(b, e1b, s["d3"], s["e1b"])
                    exp(b, e1, s["d1"], s["e1"])
                    exp(b, q_sb, s["d2"], s["e2"])
                for j in range(HC):
                    if j == J_SQ3 and Z:
                        act.wait_ge(s["center3"], at(i - 1, 1))
                        if due(at(i - 2, 1)):
                            act.wait_ge(s["half_sq3"], at(i - 2, 1))
                        nc.scalar.activation(sq3[:], x2[1 - m][:], ACT.Square).then_inc(s["sq3"], 1)
                    if j == J_SQ2 and W:
                        act.wait_ge(s["center2"], at(b, 1))
                        act.wait_ge(s["n1"], at(b, 1))
                        nc.scalar.activation(ev[:], e1b[:], ACT.Square).then_inc(s["sq2"], 1)
                    if F:
                        silu(i, j)
                act.preload_act_table_set(EXP_LN)
                if Z:
                    rstd(i - 1, st3_ps[:, 1], s["var3"], ln3, rstd3, s["ln3"], s["rstd3"], s["x3"])
                if W:
                    rstd(b, st2_ps[:, 1], s["var2"], ln2, rstd2, s["ln2"], s["rstd2"], s["x2"])
            steps(act, step)

        @block.vector
        def _(dve):
            dve.wait_ge(s["dec_exp"], 1)
            nc.vector.memset(over_d[:], 1.0 / D)
            nc.vector.memset(eps[:, 0:1], EPS * 2.0 ** -DOWN)
            nc.vector.memset(eps[:, 1:2], -0.5 * DOWN * LN_2)
            nc.vector.memset(decay_l[:], 1.0)
            nc.vector.tensor_scalar(decay[:], decay[:], -1.0, None, ALU.mult)
            nc.vector.memset(pp[:, :, 0:1], NEG)
            nc.vector.memset(aa[:, :, 0:1], 0.0)
            nc.vector.memset(bb[:, :, 0:1], 0.0).then_inc(s["const"], 1)
            dve.wait_ge(s["const"], 1)
            for c in range(DC):
                nc.vector.tensor_scalar(decay_l[:, c], decay_l[:, c], decay[:, c:c + 1], None, ALU.mult)
            nc.vector.tensor_copy(eps[:], eps[:]).then_inc(s["const"], 1)
            dve.wait_ge(s["const"], 2)

            def tt(out, a, b_, op, s_out):
                nc.vector.tensor_tensor(out, a, b_, op).then_inc(s_out, 1)

            def stt(out, a, sc, b_, op0, op1):
                return nc.vector.scalar_tensor_tensor(out, a, sc, b_, op0, op1)

            before, after = (lambda t: t[:, :, 0:L]), (lambda t: t[:, :, 1:L + 1])

            def gated(b, j):
                dve.wait_ge(s["silu"], at(b, HC, j))
                if j == 0:
                    if due(at(b - 1, 2, 1)):
                        dve.wait_ge(s["down"], at(b - 1, 2, 1))
                stt(h_sb[:, j], gu_ps[j % GU][:, 1], s_up[:, j:j + 1], g_sb[:, j % GU],
                    ALU.mult, ALU.mult).then_inc(s["h"], 1)

            def wkv(b, part):
                if part == 0:
                    dve.wait_ge(s["k_in"], at(b, 16, 15))
                    if due(at(b - 1, 1)):
                        dve.wait_ge(s["d4"], at(b - 1, 1))
                    for c in range(DC):
                        ins = nc.vector.tensor_tensor_scan(pp[:, c, 1:L + 1], decay_l[:, c], k_sb[:, c],
                                                           NEG, ALU.add, ALU.max)
                    ins.then_inc(s["pp"], 1)
                elif part == 1:
                    dve.wait_ge(s["pp"], at(b, 1))
                    for c in range(DC):
                        ins = stt(q_sb[:, c], k_sb[:, c], first[:, c:c + 1], pp[:, c, 0:L], ALU.add, ALU.max)
                    ins.then_inc(s["q"], 1)
                elif part == 2:
                    dve.wait_ge(s["q"], at(b, 1))
                    tt(e1[:], before(pp), q_sb[:], ALU.subtract, s["d1"])
                elif part == 3:
                    dve.wait_ge(s["d1"], at(b, 1))
                    for c in range(DC):
                        ins = stt(q_sb[:, c], k_sb[:, c], first[:, c:c + 1], q_sb[:, c], ALU.add, ALU.subtract)
                    ins.then_inc(s["d2"], 1)
                elif part == 4:
                    if due(at(b - 1, 1)):
                        dve.wait_ge(s["x2"], at(b - 1, 1))
                    for c in range(DC):
                        ins = stt(e1b[:, c], pp[:, c, 0:L], decay[:, c:c + 1], pp[:, c, 1:L + 1],
                                  ALU.add, ALU.subtract)
                    ins.then_inc(s["d3"], 1)
                elif part == 5:
                    dve.wait_ge(s["e1b"], at(b, 1))
                    dve.wait_ge(s["e2b"], at(b, 1))
                    for c in range(DC):
                        ins = nc.vector.tensor_tensor_scan(bb[:, c, 1:L + 1], e1b[:, c], e2b[:, c],
                                                           0.0, ALU.mult, ALU.add)
                    ins.then_inc(s["bb"], 1)
                elif part == 6:
                    dve.wait_ge(s["ev"], at(b, 1))
                    for c in range(DC):
                        ins = nc.vector.tensor_tensor_scan(aa[:, c, 1:L + 1], e1b[:, c], ev[:, c],
                                                           0.0, ALU.mult, ALU.add)
                    ins.then_inc(s["aa"], 1)
                elif part == 7:
                    dve.wait_ge(s["e2"], at(b, 1))
                    dve.wait_ge(s["bb"], at(b, 1))
                    tt(e2b[:], e1[:], before(bb), ALU.mult, s["m1"])
                    dve.wait_ge(s["m1"], at(b, 1))
                    tt(e2b[:], e2b[:], q_sb[:], ALU.add, s["den"])
                elif part == 8:
                    dve.wait_ge(s["aa"], at(b, 1))
                    tt(e1b[:], e1[:], before(aa), ALU.mult, s["n1"])
                    dve.wait_ge(s["den"], at(b, 1))
                    nc.vector.reciprocal(e2b[:], e2b[:]).then_inc(s["rec"], 1)
                elif part == 9:
                    dve.wait_ge(s["n2"], at(b, 1))
                    dve.wait_ge(s["n1"], at(b, 1))
                    tt(e1b[:], e1b[:], ev[:], ALU.add, s["num"])
                    dve.wait_ge(s["rec"], at(b, 1))
                    dve.wait_ge(s["num"], at(b, 1))
                    tt(e1b[:], e1b[:], e2b[:], ALU.mult, s["y"])
                    dve.wait_ge(s["y"], at(b, 1))
                    tt(e1b[:], e1b[:], k_sb[:], ALU.add, s["r2"])
                elif part == 10:
                    dve.wait_ge(s["mean2"], at(b, 1))
                    dve.wait_ge(s["r2"], at(b, 1))
                    dve.wait_ge(s["half_r2"], at(b, 1))
                    tt(e1b[:], e1b[:], st2_ps[:, 0:1].to_broadcast([P, DC, L]), ALU.subtract, s["center2"])

            def norm2(b, m):
                dve.wait_ge(s["rstd2"], at(b, 1))
                dve.wait_ge(s["center2"], at(b, 1))
                if not (isinstance(b, int) and b < 2):
                    dve.wait_ge(s["stored"], at(b - 2, 16, 15))
                tt(x2[m][:], e1b[:], rstd2[:].to_broadcast([P, DC, L]), ALU.mult, s["x2"])

            def residual3(b, m, j):
                dve.wait_ge(s["down"], at(b, 2, j))
                for c in (2 * j, 2 * j + 1):
                    ins = stt(x2[m][:, c], dn_ps[j][:, c % 2], s_down[:, c:c + 1], x2[m][:, c],
                              ALU.mult, ALU.add)
                ins.then_inc(s["r3"], 1)

            def step(i, m, W, F, Z):
                b = i + 1
                if isinstance(i, int) and i == 0:
                    for name, wt in (("gate", gate_w), ("up", up_w), ("down", down_w)):
                        dve.wait_ge(s["in_" + name], 16)
                        nc.vector.tensor_scalar(wt[:], wt[:].bitcast(INT32), -ZERO_POINT, None,
                                                ALU.add).then_inc(s["converted"], 1)
                if W:
                    for part in range(5):
                        wkv(b, part)
                if Z:
                    residual3(i - 1, 1 - m, 1)
                for j in range(HC):
                    if W:
                        for part in PARTS.get(j, ()):
                            wkv(b, part)
                    if j == J_CENTER3 and Z:
                        dve.wait_ge(s["mean3"], at(i - 1, 1))
                        dve.wait_ge(s["r3"], at(i - 1, 2, 1))
                        dve.wait_ge(s["half_r3"], at(i - 1, 1))
                        tt(x2[1 - m][:], x2[1 - m][:], st3_ps[:, 0:1].to_broadcast([P, DC, L]),
                           ALU.subtract, s["center3"])
                    if F:
                        gated(i, j)
                if W:
                    norm2(b, 1 - m)
                if F:
                    residual3(i, m, 0)
            steps(dve, step)

        @block.gpsimd
        def _(pool):
            def tt(out, a, b_, op, s_out):
                nc.gpsimd.tensor_tensor(out, a, b_, op).then_inc(s_out, 1)

            def halve(what, src):
                tt(sums[what][:, 0:2], src[:, 0:2], src[:, 2:4], ALU.add, s["half_" + what])

            def total(what):
                tt(sums[what][:, 2], sums[what][:, 0], sums[what][:, 1], ALU.add, s["sum_" + what])

            def step(i, m, W, F, Z):
                b = i + 1
                if W:
                    pool.wait_ge(s["pp"], at(b, 1))
                    if due(at(b - 1, 1)):
                        pool.wait_ge(s["rec"], at(b - 1, 1))
                    if due(at(b - 1, 1)):
                        pool.wait_ge(s["y"], at(b - 1, 1))
                    tt(e2b[:], k_sb[:], pp[:, :, 1:L + 1], ALU.subtract, s["d4"])
                    pool.wait_ge(s["e2b"], at(b, 1))
                    pool.wait_ge(s["v_in"], at(b, 16, 15))
                    if due(at(b - 1, 1)):
                        pool.wait_ge(s["half_sq2"], at(b - 1, 1))
                    tt(ev[:], e2b[:], v_in[:], ALU.mult, s["ev"])
                    pool.wait_ge(s["e2"], at(b, 1))
                    pool.wait_ge(s["aa"], at(b, 1))
                    tt(ev[:], q_sb[:], v_in[:], ALU.mult, s["n2"])
                if Z:
                    if due(at(i - 2, 1)):
                        pool.wait_ge(s["mean3"], at(i - 2, 1))
                    pool.wait_ge(s["r3"], at(i - 1, 2, 1))
                    halve("r3", x2[1 - m])
                    pool.wait_ge(s["half_r3"], at(i - 1, 1))
                    total("r3")
                    if due(at(i - 2, 1)):
                        pool.wait_ge(s["var3"], at(i - 2, 1))
                    pool.wait_ge(s["sq3"], at(i - 1, 1))
                    halve("sq3", sq3)
                    pool.wait_ge(s["half_sq3"], at(i - 1, 1))
                    total("sq3")
                if W:
                    if due(at(b - 1, 1)):
                        pool.wait_ge(s["mean2"], at(b - 1, 1))
                    pool.wait_ge(s["r2"], at(b, 1))
                    halve("r2", e1b)
                    pool.wait_ge(s["half_r2"], at(b, 1))
                    total("r2")
                    if due(at(b - 1, 1)):
                        pool.wait_ge(s["var2"], at(b - 1, 1))
                    pool.wait_ge(s["sq2"], at(b, 1))
                    halve("sq2", ev)
                    pool.wait_ge(s["half_sq2"], at(b, 1))
                    total("sq2")
                if Z:
                    pool.wait_ge(s["rstd3"], at(i - 1, 1))
                    tt(x2[1 - m][:], x2[1 - m][:], rstd3[:].to_broadcast([P, DC, L]), ALU.mult, s["x3"])
            steps(pool, step)

        @block.tensor
        def _(pe):
            pe.wait_ge(s["const"], 2)

            def stat(bank_half, what, b, s_out):
                pe.wait_ge(s["sum_" + what], at(b, 1))
                nc.tensor.matmul(bank_half, over_d[:], sums[what][:, 2], start=True, stop=True).then_inc(s_out, 1)

            def gate_up(b, m, j):
                if due(at(b, HC, j - GU) if j >= GU else at(b - 1, HC, HC - 1)):
                    pe.wait_ge(s["h"], at(b, HC, j - GU) if j >= GU else at(b - 1, HC, HC - 1))
                for t, wt in enumerate((gate_w, up_w)):
                    for k in range(DC):
                        ins = nc.tensor.matmul(gu_ps[j % GU][:, t], wt[:, k, j * P:(j + 1) * P], x2[m][:, k],
                                               start=(k == 0), stop=(k == DC - 1))
                ins.then_inc(s["gu"], 1)

            def down(b, j):
                if j == 0:
                    pe.wait_ge(s["h"], at(b, HC, HC - 2))
                if due(at(b - 1, 2, j)):
                    pe.wait_ge(s["r3"], at(b - 1, 2, j))
                for c in range(2):
                    ch = (2 * j + c) * P
                    for k in range(HC):
                        if j == 0 and c == 0 and k == HC - 1:
                            pe.wait_ge(s["h"], at(b, HC, HC - 1))
                        ins = nc.tensor.matmul(dn_ps[j][:, c], down_w[:, k, ch:ch + P], h_sb[:, k],
                                               start=(k == 0), stop=(k == HC - 1))
                ins.then_inc(s["down"], 1)

            def step(i, m, W, F, Z):
                b = i + 1
                if isinstance(i, int) and i == 0:
                    pe.wait_ge(s["converted"], 2)
                if F:
                    pe.wait_ge(s["x2"], at(i, 1))
                for j in range(HC):
                    if Z and j == J_MEAN3:
                        if due(at(i - 2, 1)):
                            pe.wait_ge(s["ln3"], at(i - 2, 1))
                        stat(st3_ps[:, 0], "r3", i - 1, s["mean3"])
                    if Z and j == J_VAR3:
                        stat(st3_ps[:, 1], "sq3", i - 1, s["var3"])
                    if W and j == J_MEAN2:
                        if due(at(b - 1, 1)):
                            pe.wait_ge(s["ln2"], at(b - 1, 1))
                        stat(st2_ps[:, 0], "r2", b, s["mean2"])
                    if F:
                        gate_up(i, m, j)
                if W:
                    stat(st2_ps[:, 1], "sq2", b, s["var2"])
                if isinstance(i, int) and i == 0:
                    pe.wait_ge(s["converted"], 3)
                if F:
                    down(i, 0)
                    down(i, 1)
            steps(pe, step)


def build(nc, w, out):
    x1_d = nc.dram_tensor("x1_d", [B, P, DC, L], FP32, kind="Internal").ap()
    bc_d = nc.dram_tensor("bc_d", [B, N, 2, L], FP32, kind="Internal").ap()
    pass1(nc, w["x"], w, x1_d, bc_d)
    pass2(nc, x1_d, w["ctx"], w, out)


def kernel(**inputs):
    import numpy as np
    import concourse.bacc as bacc
    from concourse.bass_utils import run_bass_kernel_spmd

    def get(name):
        return np.asarray(inputs[name])

    def cols(a):
        return a.reshape(a.shape[0], -1, P).transpose(2, 1, 0)

    def vec(a):
        return a.reshape(-1, P).T

    def rows(a):
        return a.reshape(-1, P, a.shape[1]).transpose(1, 0, 2)

    def tokens(a):
        return a.reshape(B, L, DC, P).transpose(0, 3, 2, 1)

    t, c, f = "L0_attn_", "L0_xattn_", "L0_ffn_"
    arrays = {
        "x": tokens(get("x")), "ctx": tokens(get("ctx_2048")),
        "in_w": cols(get(t + "in_w")), "skip_w": cols(get(t + "skip_w")), "wd1": cols(get(t + "wd1")),
        "wbc": cols(np.concatenate([get(t + "wB"), get(t + "wC")])), "wd2": get(t + "wd2").T,
        "out_w": cols(get(t + "out_w")), "norm_w": vec(get(t + "norm_w")), "conv_w": rows(get(t + "conv_w")),
        "conv_b": vec(get(t + "conv_b")), "wd2_b": vec(get(t + "wd2_b")), "w_d": vec(get(t + "W_D")),
        "a_log": rows(get(t + "A_log")), "decay": vec(get(c + "time_decay")), "first": vec(get(c + "time_first")),
        "gate": cols(get(f + "wq_gate")), "up": cols(get(f + "wq_up")), "down": cols(get(f + "wq_down")),
        "s_gate": vec(get(f + "s_gate")), "s_up": vec(get(f + "s_up")), "s_down": vec(get(f + "s_down")),
    }
    arrays = {n: np.ascontiguousarray(a) for n, a in arrays.items()}
    nc = bacc.Bacc("TRN2", target_bir_lowering=False, num_devices=1)
    w = {n: nc.dram_tensor("in_" + n, a.shape, mybir.dt.from_np(a.dtype), kind="ExternalInput").ap()
         for n, a in arrays.items()}
    out = nc.dram_tensor("out", (B, P, DC, L), FP32, kind="ExternalOutput").ap()
    build(nc, w, out)
    r = run_bass_kernel_spmd(nc, [{"in_" + n: a for n, a in arrays.items()}], core_ids=[0])
    return r.results[0]["out"].transpose(0, 3, 2, 1).reshape(B, L, D)
```
